# Optimizing a Trainium2 kernel written in Bass

```python
import numpy as np
import jax
import jax.numpy as jnp

def _softmax(x, axis=-1):
    return jax.nn.softmax(x, axis=axis)

def _gelu(x):
    return jax.nn.gelu(x, approximate=True)

def _silu(x):
    return jax.nn.silu(x)

def _sigmoid(x):
    return jax.nn.sigmoid(x)

def _layernorm(x, axis=-1, eps=1e-05):
    m = jnp.mean(x, axis=axis, keepdims=True)
    v = jnp.var(x, axis=axis, keepdims=True)
    return (x - m) / jnp.sqrt(v + eps)

def _scatter_add(tgt, idx, src, axis=0):
    return tgt.at[idx].add(src)

def _segment_sum(src, seg, n):
    return jax.ops.segment_sum(src, seg, n)
kernel_name = 'mk_cond_resid_d1_seqx_r2_7f8ea8'

def setup_inputs(seed: int=0):
    np.random.seed(seed)
    _w = jnp.asarray

    def _rec_inputs():
        import jax
        import jax.numpy as jnp
        _rk = jax.random.key(seed)
        x = -5.722e-05 + 0.9998 * jax.random.normal(jax.random.fold_in(_rk, 1), (2, 2048, 512), jnp.float32)
        _lenS = 2048 - jax.random.randint(jax.random.fold_in(_rk, 7), (2,), 0, max(1, 2048 // 4) + 1, jnp.int32)
        _lenS2 = 2048 - jax.random.randint(jax.random.fold_in(_rk, 8), (2,), 0, max(1, 2048 // 4) + 1, jnp.int32)
        cond_1024 = -0.0142567 + 1.00875 * jax.random.normal(jax.random.fold_in(_rk, 11), (2, 512), jnp.float32)
        return (x, cond_1024)
    x, cond_1024 = _rec_inputs()

    def _L0_cond_setup():
        import jax, jax.numpy as jnp
        import numpy as np
        MODEL_DIM = 512
        NUM_HEADS = 16
        HEAD_DIM = MODEL_DIM // NUM_HEADS
        BATCH = 16
        KEY_LEN = 2048
        key = jax.random.key(seed)
        ks = jax.random.split(key, 10)
        u = lambda k, shape: jax.random.uniform(k, shape, jnp.float32, -0.5, 0.5)
        return {'hidden_states': jax.random.normal(ks[0], (BATCH, 1, MODEL_DIM), jnp.float32), 'key_value_states': jax.random.normal(ks[1], (BATCH, KEY_LEN, MODEL_DIM), jnp.float32), 'Wq': u(ks[2], (MODEL_DIM, MODEL_DIM)), 'bq': u(ks[3], (MODEL_DIM,)), 'Wk': u(ks[4], (MODEL_DIM, MODEL_DIM)), 'bk': u(ks[5], (MODEL_DIM,)), 'Wv': u(ks[6], (MODEL_DIM, MODEL_DIM)), 'bv': u(ks[7], (MODEL_DIM,)), 'Wo': u(ks[8], (MODEL_DIM, MODEL_DIM)), 'bo': u(ks[9], (MODEL_DIM,))}
    _L0_cond_all = _L0_cond_setup()
    _L0_cond_in = {k: v for k, v in _L0_cond_all.items() if k in ('Wq', 'bq', 'Wk', 'bk', 'Wv', 'bv', 'Wo', 'bo')}
    del _L0_cond_all
    return {'x': x, 'cond_1024': cond_1024, 'L0_cond_Wq': _L0_cond_in['Wq'], 'L0_cond_bq': _L0_cond_in['bq'], 'L0_cond_Wk': _L0_cond_in['Wk'], 'L0_cond_bk': _L0_cond_in['bk'], 'L0_cond_Wv': _L0_cond_in['Wv'], 'L0_cond_bv': _L0_cond_in['bv'], 'L0_cond_Wo': _L0_cond_in['Wo'], 'L0_cond_bo': _L0_cond_in['bo']}

def reference(x, cond_1024, L0_cond_Wq, L0_cond_bq, L0_cond_Wk, L0_cond_bk, L0_cond_Wv, L0_cond_bv, L0_cond_Wo, L0_cond_bo):
    import jax
    import jax.numpy as jnp

    def _L0_cond_ref(hidden_states, key_value_states, Wq, bq, Wk, bk, Wv, bv, Wo, bo):
        import jax, jax.numpy as jnp
        import numpy as np
        MODEL_DIM = 512
        NUM_HEADS = 16
        HEAD_DIM = MODEL_DIM // NUM_HEADS
        BATCH = 16
        KEY_LEN = 2048
        B, K = (key_value_states.shape[0], key_value_states.shape[1])
        H, Dh = (NUM_HEADS, HEAD_DIM)
        q = hidden_states @ Wq.T + bq
        k = key_value_states @ Wk.T + bk
        v = key_value_states @ Wv.T + bv
        q = q.reshape(B, 1, H, Dh).transpose(0, 2, 1, 3)
        k = k.reshape(B, K, H, Dh).transpose(0, 2, 1, 3)
        v = v.reshape(B, K, H, Dh).transpose(0, 2, 1, 3)
        q = q / jnp.sqrt(jnp.asarray(Dh, q.dtype))
        scores = jnp.einsum('bhqd,bhkd->bhqk', q, k)[:, :, 0, :]
        attn = jnp.clip(scores, 0.0, 1.0)
        context = attn[..., None] * v
        context = context.transpose(0, 2, 1, 3).reshape(B, K, H * Dh)
        output = context @ Wo.T + bo
        return output
    x = x + _L0_cond_ref(cond_1024[:, None, :], x, L0_cond_Wq, L0_cond_bq, L0_cond_Wk, L0_cond_bk, L0_cond_Wv, L0_cond_bv, L0_cond_Wo, L0_cond_bo)
    return x

_drawn_inputs = setup_inputs


def setup_inputs(seed=0):
    import zlib

    import numpy as np

    out = dict(_drawn_inputs(seed))
    spreads = {}
    factors = {'L0_cond_bo': 5.945}
    for name, (base, spread) in spreads.items():
        noise = np.random.default_rng([zlib.crc32(name.encode()), seed]).standard_normal(out[name].shape)
        drawn = base * np.exp(spread * noise) if base else spread * noise
        out[name] = jnp.asarray(drawn.astype(out[name].dtype))
    for name, factor in factors.items():
        out[name] = (out[name] * factor).astype(out[name].dtype)
    return out
```

```python
from contextlib import ExitStack

import numpy as np

import concourse.bass as bass
from concourse import mybir

P = 128
BATCH = 2
LEN = 2048
D = 512
HEADS = 16
HEAD_DIM = D // HEADS
KT = D // P
MT = D // P
NT = D // P
ROWS = 512
PER_BATCH = LEN // ROWS
CHUNKS = BATCH * PER_BATCH
REP = P // HEADS
CHUNK = KT * ROWS
SCALE = float(HEAD_DIM) ** -0.5

ROW_HI, ROW_LO, ROW_SMALL = 0, HEADS, 2 * HEADS

C_SELECT = 0
C_SAME = C_SELECT + P
C_HEAD = C_SAME + P
C_LO = C_HEAD + HEADS
C_ALL = C_LO + 1

F32 = mybir.dt.float32
F32R = mybir.dt.float32r
ALU = mybir.AluOpType
ACT = mybir.ActivationFunctionType


def build(nc, x_t, wv_t, wo_t, wq_t, wk_t, cond_t, columns, constants, out_t):
    with ExitStack() as ctx:
        def sb(name, shape, dtype=F32):
            return ctx.enter_context(nc.sbuf_tensor(name, shape, dtype))

        def sem(name):
            return ctx.enter_context(nc.semaphore(name))

        x_all = sb("x_all", [P, CHUNKS * CHUNK])

        def staged(chunk):
            return x_all[:, chunk * CHUNK:(chunk + 1) * CHUNK].rearrange("p (t n) -> p t n", t=KT)

        wv_raw, wo_raw, wk_raw, wq_raw = (staged(c) for c in (4, 5, 6, 7))

        x_hi = sb("x_hi", [P, BATCH, KT, ROWS], F32R)
        x_lo = sb("x_lo", [P, BATCH, KT, ROWS], F32R)
        wv_hi = sb("wv_hi", [P, KT, D], F32R)
        wv_lo = sb("wv_lo", [P, KT, D], F32R)
        wo_hi = sb("wo_hi", [P, MT, D], F32R)
        wo_lo = sb("wo_lo", [P, MT, D], F32R)
        a_for_hi = sb("a_for_hi", [P, BATCH, KT, P], F32R)
        a_for_lo = sb("a_for_lo", [P, BATCH, KT, P], F32R)
        select = sb("select", [P, P], F32R)
        score_hi = sb("score_hi", [P, ROWS], F32R)
        score_parts = sb("score_parts", [P, ROWS], F32R)
        relu = sb("relu", [P, ROWS])
        attn = sb("attn", [P, ROWS])
        context = sb("context", [P, MT, ROWS])
        ctx_hi = sb("ctx_hi", [P, BATCH, MT, ROWS], F32R)
        ctx_lo = sb("ctx_lo", [P, BATCH, MT, ROWS], F32R)
        cond = sb("cond", [P, KT, BATCH])
        cols = sb("cols", [P, 4, MT])
        const = sb("const", [P, C_ALL])
        q_sum = sb("q_sum", [P, MT, BATCH])
        q_heads = sb("q_heads", [P, MT, BATCH, HEADS])
        bk_q = sb("bk_q", [P, MT, BATCH])
        c_score = sb("c_score", [P, BATCH])
        bq, bk, bv, bo = (cols[:, n, :] for n in range(4))

        def bank(name):
            return ctx.enter_context(nc.psum_tensor(name, [P, 512], F32))

        v_bank = [bank(f"v_bank{m}") for m in range(MT)]
        o_bank = [bank(f"o_bank{n}") for n in range(2)]
        s_bank = bank("s_bank")
        b_bank = bank("b_bank")
        q_psum = o_bank[0][:, 0:MT * BATCH].rearrange("p (m b) -> p m b", m=MT)
        c_psum = o_bank[0][:, 64:64 + BATCH]
        a_psum = o_bank[1][:, 0:KT * BATCH * HEADS].rearrange("p (k b h) -> p k b h", k=KT, b=BATCH)

        wv_loaded = [sem(f"wv_loaded{k}") for k in range(KT)]
        x0_loaded = [sem(f"x0_loaded{k}") for k in range(KT)]
        small_loaded = sem("small_loaded")
        wq_loaded = sem("wq_loaded")
        wk_loaded = sem("wk_loaded")
        wo_loaded = sem("wo_loaded")
        x_loaded = sem("x_loaded")
        stored = sem("stored")
        wv_hi_ready, wv_lo_ready = sem("wv_hi_ready"), sem("wv_lo_ready")
        wo_hi_ready, wo_lo_ready = sem("wo_hi_ready"), sem("wo_lo_ready")
        q_done, q_sum_ready, q_ready = sem("q_done"), sem("q_sum_ready"), sem("q_ready")
        a_done, c_done = sem("a_done"), sem("c_done")
        zeros_ready, a_hi_ready, a_ready = sem("zeros_ready"), sem("a_hi_ready"), sem("a_ready")
        c_ready, select_ready = sem("c_ready"), sem("select_ready")
        x_hi_ready, x_lo_ready = sem("x_hi_ready"), sem("x_lo_ready")
        score_done, score_hi_ready, score_parts_ready = sem("score_done"), sem("score_hi_ready"), sem("score_parts_ready")
        spread_done, relu_ready, attn_ready = sem("spread_done"), sem("relu_ready"), sem("attn_ready")
        v_done, context_ready = sem("v_done"), sem("context_ready")
        ctx_hi_ready, ctx_lo_ready = sem("ctx_hi_ready"), sem("ctx_lo_ready")
        o_done, out_ready = sem("o_done"), sem("out_ready")

        def wait(eng, semaphore, count):
            if not isinstance(count, int) or count > 0:
                eng.wait_ge(semaphore, count)

        def x_chunk(c, first=0, tiles=KT):
            return x_all[:, bass.ds(c * CHUNK + first * ROWS, tiles * ROWS)]

        block = ctx.enter_context(nc.Block())

        @block.sync
        def _(sp):
            for k in range(KT):
                sp.dma_start(x_chunk(0, k, 1), x_t[0, :, k * ROWS:(k + 1) * ROWS]).then_inc(x0_loaded[k], 16)
            sp.dma_start(wq_raw, wq_t).then_inc(wq_loaded, 16)
            sp.dma_start(wk_raw, wk_t).then_inc(wk_loaded, 16)
            sp.dma_start(x_chunk(1), x_t[1]).then_inc(x_loaded, 16)
            sp.wait_ge(wv_lo_ready, KT)
            sp.wait_ge(wo_lo_ready, MT)
            sp.wait_ge(a_done, 1)
            with sp.Fori(2, CHUNKS) as c:
                sp.wait_ge(x_loaded, 16 * c - 16)
                sp.dma_start(x_chunk(c), x_t[bass.ds(c, 1)].rearrange("a p n -> (a p) n")).then_inc(x_loaded, 16)
            with sp.Fori(0, CHUNKS - 1) as c:
                sp.wait_ge(out_ready, NT * c + NT)
                sp.dma_start(out_t[bass.ds(c, 1)].rearrange("a p n -> (a p) n"), x_chunk(c)).then_inc(stored, 16)
            for n in range(NT):
                sp.wait_ge(out_ready, NT * (CHUNKS - 1) + n + 1)
                sp.dma_start(out_t[CHUNKS - 1, :, n * ROWS:(n + 1) * ROWS], x_chunk(CHUNKS - 1, n, 1)).then_inc(stored, 16)
            sp.wait_ge(stored, 16 * (CHUNKS - 1 + NT))

        @block.tensor
        def _(pe):
            def product(out, w_hi, w_lo, y_hi, y_lo, first, last):
                pe.matmul(out, w_hi, y_hi, start=first, stop=False)
                pe.matmul(out, w_hi, y_lo, start=False, stop=False)
                return pe.matmul(out, w_lo, y_hi, start=False, stop=last)

            def value_tile(b, m, k):
                at = slice(m * P, (m + 1) * P)
                return product(v_bank[m][:, :], wv_hi[:, k, at], wv_lo[:, k, at],
                               x_hi[:, b, k, :], x_lo[:, b, k, :], k == 0, k == KT - 1)

            def scores(c, b):
                wait(pe, x_lo_ready, KT * c + KT)
                wait(pe, score_parts_ready, c)
                for k in range(KT):
                    pe.matmul(s_bank[:, :], a_for_hi[:, b, k, :], x_hi[:, b, k, :], start=k == 0, stop=False)
                    mm = pe.matmul(s_bank[:, :], a_for_lo[:, b, k, :], x_lo[:, b, k, :], start=False, stop=k == KT - 1)
                mm.then_inc(score_done, 1)

            def values(c, b, m):
                wait(pe, context_ready, MT * (c - 1) + m + 1)
                for k in range(KT):
                    mm = value_tile(b, m, k)
                mm.then_inc(v_done, 1)

            def spread(c):
                wait(pe, score_parts_ready, c + 1)
                wait(pe, relu_ready, c)
                pe.matmul(b_bank[:, :], select[:, :], score_parts[:, :], start=True, stop=True).then_inc(spread_done, 1)

            def outputs(c, b):
                wait(pe, ctx_lo_ready, MT * c + MT)
                for n in range(NT):
                    wait(pe, out_ready, NT * c + n - 1)
                    at = slice(n * P, (n + 1) * P)
                    for m in range(MT):
                        mm = product(o_bank[n % 2][:, :], wo_hi[:, m, at], wo_lo[:, m, at],
                                     ctx_hi[:, b, m, :], ctx_lo[:, b, m, :], m == 0, m == MT - 1)
                    mm.then_inc(o_done, 1)

            def step(c, b):
                scores(c, b)
                values(c, b, 0)
                spread(c)
                for m in range(1, MT):
                    values(c, b, m)
                outputs(c - 1, 1 - b)

            for k in range(KT):
                if k == KT - 1:
                    pe.wait_ge(wq_loaded, 16)
                    pe.wait_ge(small_loaded, 48)
                    for m in range(MT):
                        for t in range(KT):
                            mm = pe.matmul(q_psum[:, m, :], wq_raw[:, t, m * P:(m + 1) * P], cond[:, t, :],
                                           start=t == 0, stop=t == KT - 1)
                    mm.then_inc(q_done, 1)
                pe.wait_ge(wv_lo_ready, k + 1)
                pe.wait_ge(x_lo_ready, k + 1)
                for m in range(MT):
                    mm = value_tile(0, m, k)
                    if k == KT - 1:
                        mm.then_inc(v_done, 1)
            pe.wait_ge(wk_loaded, 16)
            pe.wait_ge(q_ready, 2)
            for k in range(KT):
                for m in range(MT):
                    mm = pe.matmul(a_psum[:, k, :, :], wk_raw[:, m, k * P:(k + 1) * P], q_heads[:, m, :, :],
                                   start=m == 0, stop=m == MT - 1)
            mm.then_inc(a_done, 1)
            for m in range(MT):
                mm = pe.matmul(c_psum, const[:, C_SAME:C_SAME + P], bk_q[:, m, :], start=m == 0, stop=m == MT - 1)
            mm.then_inc(c_done, 1)
            pe.wait_ge(a_ready, 2 * BATCH)
            scores(0, 0)
            pe.wait_ge(select_ready, 1)
            spread(0)
            pe.wait_ge(c_ready, 1)
            pe.wait_ge(wo_lo_ready, MT)
            step(1, 1)
            with pe.Fori(0, PER_BATCH - 1) as i:
                for b in range(BATCH):
                    step(2 * i + 2 + b, b)
            outputs(CHUNKS - 1, 1)

        @block.scalar
        def _(act):
            for k in range(KT):
                act.dma_start(wv_raw[:, k, :], wv_t[:, k, :]).then_inc(wv_loaded[k], 16)
            for to, of in ((cond[:, :, :], cond_t), (cols[:, :, :], columns), (const[:, :], constants)):
                act.dma_start(to, of).then_inc(small_loaded, 16)
            act.dma_start(wo_raw, wo_t).then_inc(wo_loaded, 16)
            for k in range(KT):
                act.wait_ge(wv_loaded[k], 16)
                nc.scalar.copy(wv_hi[:, k, :], wv_raw[:, k, :]).then_inc(wv_hi_ready, 1)
            act.wait_ge(wo_loaded, 16)
            for m in range(MT):
                nc.scalar.copy(wo_hi[:, m, :], wo_raw[:, m, :]).then_inc(wo_hi_ready, 1)
            act.wait_ge(c_ready, 1)

            def step(c, b):
                wait(act, score_done, c + 1)
                wait(act, score_parts_ready, c)
                nc.scalar.copy(score_hi[:, :], s_bank[:, :]).then_inc(score_hi_ready, 1)
                wait(act, spread_done, c + 1)
                wait(act, attn_ready, c)
                nc.scalar.activation(relu[:, :], b_bank[:, :], ACT.Relu, bias=c_score[:, b:b + 1]).then_inc(relu_ready, 1)
                for m in range(MT):
                    wait(act, context_ready, MT * c + m + 1)
                    if m == 0:
                        wait(act, o_done, NT * (c - 1))
                    nc.scalar.copy(ctx_hi[:, b, m, :], context[:, m, :]).then_inc(ctx_hi_ready, 1)

            step(0, 0)
            step(1, 1)
            with act.Fori(0, PER_BATCH - 1) as i:
                for b in range(BATCH):
                    step(2 * i + 2 + b, b)

        @block.gpsimd
        def _(pool):
            for k in range(KT):
                pool.wait_ge(x0_loaded[k], 16)
                nc.gpsimd.tensor_copy(x_hi[:, 0, k, :], x_chunk(0, k, 1)).then_inc(x_hi_ready, 1)
            nc.gpsimd.memset(a_for_hi[:, :, :, :].bitcast(F32), 0.0).then_inc(zeros_ready, 1)
            nc.gpsimd.memset(a_for_lo[:, :, :, :].bitcast(F32), 0.0).then_inc(zeros_ready, 1)
            pool.wait_ge(small_loaded, 48)
            nc.gpsimd.tensor_copy(select[:, :], const[:, C_SELECT:C_SELECT + P]).then_inc(select_ready, 1)

            def hi_of_x(c, b):
                pool.wait_ge(x_loaded, 16 * c)
                wait(pool, v_done, MT * (c - 1))
                nc.gpsimd.tensor_copy(x_hi[:, b, :, :], x_chunk(c)).then_inc(x_hi_ready, KT)

            hi_of_x(1, 1)
            with pool.Fori(0, PER_BATCH - 1) as i:
                for b in range(BATCH):
                    hi_of_x(2 * i + 2 + b, b)

        @block.vector
        def _(dve):
            def lo_part(to, of, hi):
                return nc.vector.tensor_tensor(to, of, hi.bitcast(F32), ALU.subtract)

            for k in range(KT):
                dve.wait_ge(wv_hi_ready, k + 1)
                lo_part(wv_lo[:, k, :], wv_raw[:, k, :], wv_hi[:, k, :]).then_inc(wv_lo_ready, 1)
                dve.wait_ge(x_hi_ready, k + 1)
                lo_part(x_lo[:, 0, k, :], x_chunk(0, k, 1), x_hi[:, 0, k, :]).then_inc(x_lo_ready, 1)
            dve.wait_ge(q_done, 1)
            dve.wait_ge(small_loaded, 48)
            nc.vector.tensor_tensor(q_sum[:, :, :], q_psum, bq.unsqueeze(2).to_broadcast([P, MT, BATCH]),
                                    ALU.add).then_inc(q_sum_ready, 1)
            dve.wait_ge(q_sum_ready, 1)
            nc.vector.scalar_tensor_tensor(
                out=q_heads[:, :, :, :].rearrange("p m b h -> p (m b) h"),
                in0=q_sum[:, :, :].rearrange("p m b -> p (m b)").unsqueeze(2).to_broadcast([P, MT * BATCH, HEADS]),
                scalar=SCALE, in1=const[:, C_HEAD:C_HEAD + HEADS].unsqueeze(1).to_broadcast([P, MT * BATCH, HEADS]),
                op0=ALU.mult, op1=ALU.mult).then_inc(q_ready, 1)
            nc.vector.scalar_tensor_tensor(
                out=bk_q[:, :, :], in0=q_sum[:, :, :], scalar=SCALE,
                in1=bk.unsqueeze(2).to_broadcast([P, MT, BATCH]), op0=ALU.mult, op1=ALU.mult).then_inc(q_ready, 1)
            dve.wait_ge(a_done, 1)
            dve.wait_ge(zeros_ready, 2)
            for b in range(BATCH):
                a = a_psum[:, :, b, :]
                hi = a_for_hi[:, b, :, ROW_HI:ROW_HI + HEADS]
                nc.vector.tensor_copy(hi, a).then_inc(a_hi_ready, 1)
                nc.vector.tensor_copy(a_for_hi[:, b, :, ROW_LO:ROW_LO + HEADS], a)
                nc.vector.tensor_copy(a_for_lo[:, b, :, ROW_HI:ROW_HI + HEADS], a)
                nc.vector.tensor_copy(a_for_lo[:, b, :, ROW_LO:ROW_LO + HEADS], a).then_inc(a_ready, 1)
                dve.wait_ge(a_hi_ready, b + 1)
                lo_part(a_for_hi[:, b, :, ROW_SMALL:ROW_SMALL + HEADS], a, hi).then_inc(a_ready, 1)
            dve.wait_ge(c_done, 1)
            nc.vector.tensor_copy(c_score[:, :], c_psum).then_inc(c_ready, 1)

            def split_scores(c):
                wait(dve, score_hi_ready, c + 1)
                wait(dve, spread_done, c)
                nc.vector.scalar_tensor_tensor(
                    out=score_parts[:, :], in0=score_hi[:, :].bitcast(F32), scalar=const[:, C_LO:C_LO + 1],
                    in1=s_bank[:, :], op0=ALU.mult, op1=ALU.add).then_inc(score_parts_ready, 1)

            def lo_of_context(c, b, m):
                wait(dve, ctx_hi_ready, MT * c + m + 1)
                lo_part(ctx_lo[:, b, m, :], context[:, m, :], ctx_hi[:, b, m, :]).then_inc(ctx_lo_ready, 1)

            def contexts(c, b):
                wait(dve, relu_ready, c + 1)
                nc.vector.tensor_scalar(attn[:, :], relu[:, :], 1.0, None, ALU.min).then_inc(attn_ready, 1)
                wait(dve, attn_ready, c + 1)
                for m in range(MT):
                    wait(dve, v_done, MT * c + m + 1)
                    nc.vector.scalar_tensor_tensor(
                        out=context[:, m, :], in0=v_bank[m][:, :], scalar=bv[:, m:m + 1], in1=attn[:, :],
                        op0=ALU.add, op1=ALU.mult).then_inc(context_ready, 1)
                    if m >= 1:
                        lo_of_context(c, b, m - 1)
                lo_of_context(c, b, MT - 1)

            def add_outputs(c):
                for n in range(NT):
                    wait(dve, o_done, NT * c + n + 1)
                    x_tile = x_chunk(c, n, 1)
                    nc.vector.scalar_tensor_tensor(
                        out=x_tile, in0=o_bank[n % 2][:, :], scalar=bo[:, n:n + 1], in1=x_tile,
                        op0=ALU.add, op1=ALU.add).then_inc(out_ready, 1)

            def lo_of_x(c, b):
                wait(dve, x_hi_ready, KT * c + KT)
                lo_part(x_lo[:, b, :, :], x_chunk(c), x_hi[:, b, :, :]).then_inc(x_lo_ready, KT)

            split_scores(0)
            for m in range(MT):
                dve.wait_ge(wo_hi_ready, m + 1)
                lo_part(wo_lo[:, m, :], wo_raw[:, m, :], wo_hi[:, m, :]).then_inc(wo_lo_ready, 1)
            lo_of_x(1, 1)
            contexts(0, 0)
            split_scores(1)
            contexts(1, 1)
            with dve.Fori(0, PER_BATCH - 1) as i:
                for b in range(BATCH):
                    c = 2 * i + 2 + b
                    lo_of_x(c, b)
                    add_outputs(c - 2)
                    split_scores(c)
                    contexts(c, b)
            add_outputs(CHUNKS - 2)
            add_outputs(CHUNKS - 1)


def constant_columns():
    const = np.zeros((P, C_ALL), np.float32)
    p = np.arange(P)
    head = p // REP
    for first in (ROW_HI, ROW_LO, ROW_SMALL):
        const[first:first + HEADS, C_SELECT:C_SELECT + P] = np.arange(HEADS)[:, None] == head[None, :]
    const[:, C_SAME:C_SAME + P] = head[:, None] == head[None, :]
    const[:, C_HEAD:C_HEAD + HEADS] = head[:, None] == np.arange(HEADS)[None, :]
    const[ROW_LO:ROW_LO + HEADS, C_LO] = -1.0
    return const


def by_value_tile(w):
    w = w.reshape(HEADS, MT, REP, *w.shape[1:])
    return np.moveaxis(w, 1, 2).reshape(P, MT, *w.shape[3:])


def kernel(x, cond_1024, L0_cond_Wq, L0_cond_bq, L0_cond_Wk, L0_cond_bk, L0_cond_Wv, L0_cond_bv, L0_cond_Wo,
           L0_cond_bo):
    import concourse.bacc as bacc
    from concourse.bass_utils import run_bass_kernel_spmd

    x, cond, Wq, bq, Wk, bk, Wv, bv, Wo, bo = (
        np.asarray(a) for a in (x, cond_1024, L0_cond_Wq, L0_cond_bq, L0_cond_Wk, L0_cond_bk, L0_cond_Wv,
                                L0_cond_bv, L0_cond_Wo, L0_cond_bo))

    def in_by_out(w):
        w = by_value_tile(w).reshape(P, MT, KT, P)
        return w.transpose(3, 2, 1, 0).reshape(P, KT, D)

    laid = {
        "x_t": x.reshape(BATCH, PER_BATCH, ROWS, KT, P).transpose(1, 0, 4, 3, 2).reshape(CHUNKS, P, CHUNK),
        "wv_t": in_by_out(Wv),
        "wo_t": by_value_tile(Wo.T),
        "wq_t": in_by_out(Wq),
        "wk_t": by_value_tile(Wk),
        "cond_t": cond.reshape(BATCH, KT, P).transpose(2, 1, 0),
        "columns": np.stack([by_value_tile(bq), by_value_tile(bk), by_value_tile(bv), bo.reshape(NT, P).T], axis=1),
        "constants": constant_columns(),
    }
    laid = {name: np.ascontiguousarray(a) for name, a in laid.items()}
    nc = bacc.Bacc("TRN2", target_bir_lowering=False, num_devices=1)
    ins = [nc.dram_tensor(name, a.shape, mybir.dt.from_np(a.dtype), kind="ExternalInput").ap()
           for name, a in laid.items()]
    out = nc.dram_tensor("out_t", (CHUNKS, P, CHUNK), F32, kind="ExternalOutput").ap()
    build(nc, *ins, out)
    r = run_bass_kernel_spmd(nc, [laid], core_ids=[0])
    out = r.results[0]["out_t"].reshape(PER_BATCH, BATCH, P, NT, ROWS)
    return out.transpose(1, 0, 4, 3, 2).reshape(BATCH, LEN, D)
```

```python
from contextlib import ExitStack

import numpy as np

import concourse.bass as bass
from concourse import mybir

P = 128
BATCH = 2
LEN = 2048
D = 512
HEADS = 16
HEAD_DIM = D // HEADS
KT = D // P
MT = D // P
NT = D // P
ROWS = 512
PER_BATCH = LEN // ROWS
CHUNKS = BATCH * PER_BATCH
REP = P // HEADS
CHUNK = KT * ROWS
WARM_UP = 9
SCALE = float(HEAD_DIM) ** -0.5

ROW_HI, ROW_LO, ROW_SMALL = 0, HEADS, 2 * HEADS

C_SELECT = 0
C_SAME = C_SELECT + P
C_HEAD = C_SAME + P
C_LO = C_HEAD + HEADS
C_FOLD = C_LO + 1
C_PAIR = C_FOLD + BATCH * HEADS
C_ALL = C_PAIR + BATCH

F32 = mybir.dt.float32
F32R = mybir.dt.float32r
ALU = mybir.AluOpType
ACT = mybir.ActivationFunctionType


def build(nc, x_t, wv_t, wo_t, wq_t, wk_t, cond_t, columns, constants, out_t):
    with ExitStack() as ctx:
        def sb(name, shape, dtype=F32):
            return ctx.enter_context(nc.sbuf_tensor(name, shape, dtype))

        def sem(name):
            return ctx.enter_context(nc.semaphore(name))

        x_all = sb("x_all", [P, CHUNKS * CHUNK])

        def staged(chunk):
            return x_all[:, chunk * CHUNK:(chunk + 1) * CHUNK].rearrange("p (t n) -> p t n", t=KT)

        wv_raw, wo_raw, wk_raw, wq_raw = (staged(c) for c in (4, 5, 6, 7))

        x_hi = sb("x_hi", [P, BATCH, KT, ROWS], F32R)
        x_lo = sb("x_lo", [P, BATCH, KT, ROWS], F32R)
        wv_hi = sb("wv_hi", [P, KT, D], F32R)
        wv_lo = sb("wv_lo", [P, KT, D], F32R)
        wo_hi = sb("wo_hi", [P, MT, D], F32R)
        wo_lo = sb("wo_lo", [P, MT, D], F32R)
        a_for_hi = sb("a_for_hi", [P, BATCH, KT, P], F32R)
        a_for_lo = sb("a_for_lo", [P, BATCH, KT, P], F32R)
        select = sb("select", [P, P], F32R)
        score_hi = sb("score_hi", [P, ROWS], F32R)
        score_parts = sb("score_parts", [P, ROWS], F32R)
        relu = sb("relu", [P, ROWS])
        attn = sb("attn", [P, ROWS])
        context = sb("context", [P, MT, ROWS])
        ctx_hi = sb("ctx_hi", [P, BATCH, MT, ROWS], F32R)
        ctx_lo = sb("ctx_lo", [P, BATCH, MT, ROWS], F32R)
        wq_hi, wq_lo = ctx_hi[:, 0, :, :], ctx_lo[:, 0, :, :]
        wk_hi, wk_lo = ctx_hi[:, 1, :, :], ctx_lo[:, 1, :, :]
        cond = sb("cond", [P, KT, BATCH])
        cond_parts = sb("cond_parts", [P, KT, P], F32R)
        q_rows = sb("q_rows", [P, D])
        warm = context[:, 0, :].bitcast(mybir.dt.bfloat16)
        cols = sb("cols", [P, 4, MT])
        const = sb("const", [P, C_ALL])
        q_sum = sb("q_sum", [P, MT, BATCH])
        q_heads = sb("q_heads", [P, MT, BATCH * HEADS])
        q_parts = sb("q_parts", [P, MT, P], F32R)
        a_rows = sb("a_rows", [P, D])
        bk_q = sb("bk_q", [P, MT, BATCH])
        c_score = sb("c_score", [P, BATCH])
        bq, bk, bv, bo = (cols[:, n, :] for n in range(4))

        def bank(name):
            return ctx.enter_context(nc.psum_tensor(name, [P, 512], F32))

        v_bank = [bank(f"v_bank{m}") for m in range(MT)]
        o_bank = [bank(f"o_bank{n}") for n in range(2)]
        score_bank = [bank(f"score_bank{b}") for b in range(BATCH)]
        a_psum = o_bank[1][:, 0:KT * BATCH * HEADS].rearrange("p (k n) -> p k n", k=KT)
        q_rows_psum, a_rows_psum = score_bank
        q_psum = o_bank[0][:, 64:64 + MT * BATCH].rearrange("p (m b) -> p m b", m=MT)
        c_psum = o_bank[0][:, 0:MT * BATCH].rearrange("p (m b) -> p m b", m=MT)

        wv_loaded = [sem(f"wv_loaded{k}") for k in range(KT)]
        x0_loaded = [sem(f"x0_loaded{k}") for k in range(KT)]
        small_loaded = sem("small_loaded")
        wq_loaded = [sem(f"wq_loaded{k}") for k in range(KT)]
        wk_loaded = [sem(f"wk_loaded{m}") for m in range(MT)]
        wo_loaded = sem("wo_loaded")
        x_loaded = sem("x_loaded")
        stored = sem("stored")
        wv_hi_ready, wv_lo_ready = sem("wv_hi_ready"), sem("wv_lo_ready")
        wo_hi_ready, wo_lo_ready = sem("wo_hi_ready"), sem("wo_lo_ready")
        warm_ready = sem("warm_ready")
        wk_hi_ready, wk_lo_ready = sem("wk_hi_ready"), sem("wk_lo_ready")
        wq_hi_ready, wq_lo_ready = sem("wq_hi_ready"), sem("wq_lo_ready")
        cond_hi_ready, cond_ready = sem("cond_hi_ready"), sem("cond_ready")
        q_rows_done, q_rows_ready, q_done = sem("q_rows_done"), sem("q_rows_ready"), sem("q_done")
        q_hi_ready, q_parts_ready = sem("q_hi_ready"), sem("q_parts_ready")
        a_rows_done, a_rows_ready = sem("a_rows_done"), sem("a_rows_ready")
        q_sum_ready, q_ready = sem("q_sum_ready"), sem("q_ready")
        a_done, c_done = sem("a_done"), sem("c_done")
        zeros_ready, a_hi_ready, a_ready = sem("zeros_ready"), sem("a_hi_ready"), sem("a_ready")
        c_ready, select_ready = sem("c_ready"), sem("select_ready")
        x0_hi_ready = sem("x0_hi_ready")
        x0_lo_ready = sem("x0_lo_ready")
        x_hi_ready = sem("x_hi_ready")
        x_lo_ready = sem("x_lo_ready")
        score_done, score_hi_ready, score_parts_ready = sem("score_done"), sem("score_hi_ready"), sem("score_parts_ready")
        spread_done, relu_ready, attn_ready = sem("spread_done"), sem("relu_ready"), sem("attn_ready")
        v_done, context_ready = sem("v_done"), sem("context_ready")
        ctx_hi_ready, ctx_lo_ready = sem("ctx_hi_ready"), sem("ctx_lo_ready")
        o_done, out_ready = sem("o_done"), sem("out_ready")

        def wait(eng, semaphore, count):
            if not isinstance(count, int) or count > 0:
                eng.wait_ge(semaphore, count)

        def x_chunk(c, first=0, tiles=KT):
            return x_all[:, bass.ds(c * CHUNK + first * ROWS, tiles * ROWS)]

        block = ctx.enter_context(nc.Block())

        @block.sync
        def _(sp):
            def x0_and_wv(k):
                sp.dma_start(x_chunk(0, k, 1), x_t[0, :, k * ROWS:(k + 1) * ROWS]).then_inc(x0_loaded[k], 16)
                sp.dma_start(wv_raw[:, k, :], wv_t[:, k, :]).then_inc(wv_loaded[k], 16)

            x0_and_wv(0)
            x0_and_wv(1)
            for to, of in ((cond[:, :, :], cond_t), (cols[:, :, :], columns), (const[:, :], constants)):
                sp.dma_start(to, of).then_inc(small_loaded, 16)
            for k in range(KT):
                sp.dma_start(wq_raw[:, k, :], wq_t[:, k, :]).then_inc(wq_loaded[k], 16)
            x0_and_wv(2)
            for m in range(MT):
                sp.dma_start(wk_raw[:, m, :], wk_t[:, m, :]).then_inc(wk_loaded[m], 16)
            x0_and_wv(3)
            sp.dma_start(x_chunk(1), x_t[1]).then_inc(x_loaded, 16)
            sp.dma_start(wo_raw, wo_t).then_inc(wo_loaded, 16)
            sp.wait_ge(wv_lo_ready, KT)
            sp.wait_ge(wo_lo_ready, MT)
            sp.wait_ge(wk_lo_ready, MT)
            with sp.Fori(2, CHUNKS) as c:
                sp.wait_ge(x_loaded, 16 * c - 16)
                sp.dma_start(x_chunk(c), x_t[bass.ds(c, 1)].rearrange("a p n -> (a p) n")).then_inc(x_loaded, 16)
            with sp.Fori(0, CHUNKS - 1) as c:
                sp.wait_ge(out_ready, NT * c + NT)
                sp.dma_start(out_t[bass.ds(c, 1)].rearrange("a p n -> (a p) n"), x_chunk(c)).then_inc(stored, 16)
            for n in range(NT - 1):
                sp.wait_ge(out_ready, NT * (CHUNKS - 1) + n + 1)
                sp.dma_start(out_t[CHUNKS - 1, :, n * ROWS:(n + 1) * ROWS], x_chunk(CHUNKS - 1, n, 1)).then_inc(stored, 16)
            for half in range(2):
                sp.wait_ge(out_ready, NT * CHUNKS + half)
                at = (NT - 1) * ROWS + half * ROWS // 2
                sp.dma_start(out_t[CHUNKS - 1, :, at:at + ROWS // 2],
                             x_all[:, bass.ds((CHUNKS - 1) * CHUNK + at, ROWS // 2)]).then_inc(stored, 16)
            sp.wait_ge(stored, 16 * (CHUNKS + NT))

        @block.tensor
        def _(pe):
            def product(out, w_hi, w_lo, y_hi, y_lo, first, last):
                pe.matmul(out, w_hi, y_hi, start=first, stop=False)
                pe.matmul(out, w_hi, y_lo, start=False, stop=False)
                return pe.matmul(out, w_lo, y_hi, start=False, stop=last)

            def value_tile(b, m, k):
                at = slice(m * P, (m + 1) * P)
                return product(v_bank[m][:, :], wv_hi[:, k, at], wv_lo[:, k, at],
                               x_hi[:, b, k, :], x_lo[:, b, k, :], k == 0, k == KT - 1)

            def scores(c, b):
                wait(pe, x_lo_ready, 2 * c)
                wait(pe, relu_ready, c - 1)
                bank = score_bank[b][:, :]
                for k in range(KT):
                    pe.matmul(bank, a_for_hi[:, b, k, :], x_hi[:, b, k, :], start=k == 0, stop=False)
                    mm = pe.matmul(bank, a_for_lo[:, b, k, :], x_lo[:, b, k, :], start=False, stop=k == KT - 1)
                mm.then_inc(score_done, 1)

            def values(c, b, m):
                wait(pe, context_ready, MT * (c - 1) + m + 1)
                for k in range(KT):
                    mm = value_tile(b, m, k)
                mm.then_inc(v_done, 1)

            def spread(c, b):
                wait(pe, score_parts_ready, c + 1)
                pe.matmul(score_bank[b][:, :], select[:, :], score_parts[:, :], start=True, stop=True).then_inc(spread_done, 1)

            def outputs(c, b, tiles=NT):
                if isinstance(c, int) and c == 0:
                    pe.wait_ge(wo_lo_ready, MT)
                wait(pe, ctx_lo_ready, MT * c + MT)
                for n in range(tiles):
                    wait(pe, out_ready, NT * c + n - 1)
                    at = slice(n * P, (n + 1) * P)
                    for m in range(MT):
                        mm = product(o_bank[n % 2][:, :], wo_hi[:, m, at], wo_lo[:, m, at],
                                     ctx_hi[:, b, m, :], ctx_lo[:, b, m, :], m == 0, m == MT - 1)
                    mm.then_inc(o_done, 1)

            def step(c, b):
                if not isinstance(c, int) or c > 1:
                    scores(c, b)
                values(c, b, 0)
                spread(c, b)
                for m in range(1, MT):
                    values(c, b, m)
                outputs(c - 1, 1 - b)

            def first_values(k, kinds=range(3)):
                for kind in kinds:
                    w, y = ((wv_hi, x_hi), (wv_hi, x_lo), (wv_lo, x_hi))[kind]
                    for part in ((x0_hi_ready, wv_hi_ready), (x0_lo_ready,), (wv_lo_ready,))[kind]:
                        pe.wait_ge(part, k + 1)
                    for m in range(MT):
                        last = k == KT - 1 and kind == 2
                        mm = pe.matmul(v_bank[m][:, :], w[:, k, m * P:(m + 1) * P], y[:, 0, k, :],
                                       start=k == 0 and kind == 0, stop=last)
                        if last:
                            mm.then_inc(v_done, 1)

            def rows(out, vectors, w_hi, w_lo, hi_ready, lo_ready):
                pe.wait_ge(hi_ready, KT)
                for k in range(KT):
                    pe.matmul(out[:, :], vectors[:, k, :], w_hi[:, k, :], start=k == 0, stop=False)
                pe.wait_ge(lo_ready, KT)
                for k in range(KT):
                    mm = pe.matmul(out[:, :], vectors[:, k, :], w_lo[:, k, :], start=False, stop=k == KT - 1)
                return mm

            pe.wait_ge(warm_ready, 1)
            for _ in range(WARM_UP):
                pe.matmul(o_bank[1][:, :], warm[:, 0:P], warm[:, 0:ROWS], start=True, stop=True)

            first_values(0)
            first_values(1)
            pe.wait_ge(cond_ready, 1)
            rows(q_rows_psum, cond_parts, wq_hi, wq_lo, wq_hi_ready, wq_lo_ready).then_inc(q_rows_done, 1)
            first_values(2, (0, 1))
            pe.wait_ge(q_rows_ready, 1)
            for m in range(MT):
                mm = pe.matmul(q_psum[:, m, :], q_rows[:, m * P:(m + 1) * P], const[:, C_PAIR:C_PAIR + BATCH],
                               start=True, stop=True)
            mm.then_inc(q_done, 1)
            first_values(2, (2,))
            pe.wait_ge(q_parts_ready, 1)
            rows(a_rows_psum, q_parts, wk_hi, wk_lo, wk_hi_ready, wk_lo_ready).then_inc(a_rows_done, 1)
            first_values(3, (0,))
            pe.wait_ge(a_rows_ready, 1)
            for k in range(KT):
                mm = pe.matmul(a_psum[:, k, :], a_rows[:, k * P:(k + 1) * P], const[:, C_FOLD:C_FOLD + BATCH * HEADS],
                               start=True, stop=True)
            mm.then_inc(a_done, 1)
            pe.wait_ge(q_ready, 2)
            pe.matmul(c_psum, const[:, C_SAME:C_SAME + P], bk_q[:, :, :], start=True, stop=True).then_inc(c_done, 1)
            first_values(3, (1,))
            pe.wait_ge(a_ready, 3)
            scores(0, 0)
            pe.wait_ge(a_ready, 3 * BATCH)
            scores(1, 1)
            pe.wait_ge(select_ready, 1)
            spread(0, 0)
            first_values(3, (2,))
            pe.wait_ge(c_ready, 1)
            step(1, 1)
            with pe.Fori(0, PER_BATCH - 1) as i:
                for b in range(BATCH):
                    step(2 * i + 2 + b, b)
            outputs(CHUNKS - 1, 1, NT - 1)
            for half in range(2):
                pe.wait_ge(out_ready, NT * CHUNKS - 2 + half)
                at, cols_at = slice((NT - 1) * P, D), slice(half * ROWS // 2, (half + 1) * ROWS // 2)
                for m in range(MT):
                    mm = product(o_bank[1 - half][:, 0:ROWS // 2], wo_hi[:, m, at], wo_lo[:, m, at],
                                 ctx_hi[:, 1, m, cols_at], ctx_lo[:, 1, m, cols_at], m == 0, m == MT - 1)
                mm.then_inc(o_done, 1)

        @block.scalar
        def _(act):
            def first_hi(k):
                act.wait_ge(x0_loaded[k], 16)
                nc.scalar.copy(x_hi[:, 0, k, :], x_chunk(0, k, 1)).then_inc(x0_hi_ready, 1)
                act.wait_ge(wv_loaded[k], 16)
                nc.scalar.copy(wv_hi[:, k, :], wv_raw[:, k, :]).then_inc(wv_hi_ready, 1)

            def hi_of_x(c, b, half):
                if half == 0:
                    act.wait_ge(x_loaded, 16 * c)
                    wait(act, v_done, MT * (c - 1))
                first = half * KT // 2
                nc.scalar.copy(x_hi[:, b, first:first + KT // 2, :].rearrange("p k n -> p (k n)"),
                               x_chunk(c, first, KT // 2)).then_inc(x_hi_ready, 1)

            def round_scores(c, b):
                wait(act, score_done, c + 1)
                wait(act, score_parts_ready, c)
                nc.scalar.copy(score_hi[:, :], score_bank[b][:, :]).then_inc(score_hi_ready, 1)

            def relu_scores(c, b):
                wait(act, spread_done, c + 1)
                wait(act, attn_ready, c)
                nc.scalar.activation(relu[:, :], score_bank[b][:, :], ACT.Relu, bias=c_score[:, b:b + 1]).then_inc(relu_ready, 1)

            def hi_of_context(c, b, m):
                wait(act, context_ready, MT * c + m + 1)
                if m == 0:
                    wait(act, o_done, NT * (c - 1))
                nc.scalar.copy(ctx_hi[:, b, m, :], context[:, m, :]).then_inc(ctx_hi_ready, 1)

            first_hi(0)
            first_hi(1)
            for k in range(KT):
                act.wait_ge(wq_loaded[k], 16)
                nc.scalar.copy(wq_hi[:, k, :], wq_raw[:, k, :]).then_inc(wq_hi_ready, 1)
            first_hi(2)
            for m in range(MT):
                act.wait_ge(wk_loaded[m], 16)
                nc.scalar.copy(wk_hi[:, m, :], wk_raw[:, m, :]).then_inc(wk_hi_ready, 1)
            act.wait_ge(q_rows_done, 1)
            nc.scalar.copy(q_rows[:, :], q_rows_psum[:, :]).then_inc(q_rows_ready, 1)
            first_hi(3)
            hi_of_x(1, 1, 0)
            act.wait_ge(a_rows_done, 1)
            nc.scalar.copy(a_rows[:, :], a_rows_psum[:, :]).then_inc(a_rows_ready, 1)
            hi_of_x(1, 1, 1)
            round_scores(0, 0)
            act.wait_ge(c_ready, 1)
            relu_scores(0, 0)
            hi_of_context(0, 0, 0)
            round_scores(1, 1)
            for m in range(1, MT):
                hi_of_context(0, 0, m)
            act.wait_ge(wo_loaded, 16)
            for m in range(MT):
                nc.scalar.copy(wo_hi[:, m, :], wo_raw[:, m, :]).then_inc(wo_hi_ready, 1)
            relu_scores(1, 1)
            for m in range(MT):
                hi_of_context(1, 1, m)
            with act.Fori(0, PER_BATCH - 1) as i:
                for b in range(BATCH):
                    c = 2 * i + 2 + b
                    hi_of_x(c, b, 0)
                    hi_of_x(c, b, 1)
                    round_scores(c, b)
                    relu_scores(c, b)
                    for m in range(MT):
                        hi_of_context(c, b, m)

        @block.gpsimd
        def _(pool):
            nc.gpsimd.memset(a_for_hi[:, :, :, :].bitcast(F32), 0.0).then_inc(zeros_ready, 1)
            nc.gpsimd.memset(a_for_lo[:, :, :, :].bitcast(F32), 0.0).then_inc(zeros_ready, 1)
            nc.gpsimd.memset(cond_parts[:, :, :].bitcast(F32), 0.0).then_inc(zeros_ready, 1)
            nc.gpsimd.memset(q_parts[:, :, :].bitcast(F32), 0.0).then_inc(zeros_ready, 1)
            pool.wait_ge(small_loaded, 48)
            nc.gpsimd.tensor_copy(select[:, :], const[:, C_SELECT:C_SELECT + P]).then_inc(select_ready, 1)

        @block.vector
        def _(dve):
            def lo_part(to, of, hi):
                return nc.vector.tensor_tensor(to, of, hi.bitcast(F32), ALU.subtract)

            def first_lo(k):
                dve.wait_ge(x0_hi_ready, k + 1)
                lo_part(x_lo[:, 0, k, :], x_chunk(0, k, 1), x_hi[:, 0, k, :]).then_inc(x0_lo_ready, 1)
                dve.wait_ge(wv_hi_ready, k + 1)
                lo_part(wv_lo[:, k, :], wv_raw[:, k, :], wv_hi[:, k, :]).then_inc(wv_lo_ready, 1)

            def lo_of_x(c, b, half):
                wait(dve, x_hi_ready, 2 * c - 1 + half)
                first = half * KT // 2
                lo_part(x_lo[:, b, first:first + KT // 2, :], x_chunk(c, first, KT // 2),
                        x_hi[:, b, first:first + KT // 2, :]).then_inc(x_lo_ready, 1)

            def split_scores(c, b):
                wait(dve, score_hi_ready, c + 1)
                wait(dve, spread_done, c)
                nc.vector.scalar_tensor_tensor(
                    out=score_parts[:, :], in0=score_hi[:, :].bitcast(F32), scalar=const[:, C_LO:C_LO + 1],
                    in1=score_bank[b][:, :], op0=ALU.mult, op1=ALU.add).then_inc(score_parts_ready, 1)

            def lo_of_context(c, b, m):
                wait(dve, ctx_hi_ready, MT * c + m + 1)
                lo_part(ctx_lo[:, b, m, :], context[:, m, :], ctx_hi[:, b, m, :]).then_inc(ctx_lo_ready, 1)

            def clip_scores(c):
                wait(dve, relu_ready, c + 1)
                nc.vector.tensor_scalar(attn[:, :], relu[:, :], 1.0, None, ALU.min).then_inc(attn_ready, 1)
                wait(dve, attn_ready, c + 1)

            def context_tile(c, b, m):
                wait(dve, v_done, MT * c + m + 1)
                nc.vector.scalar_tensor_tensor(
                    out=context[:, m, :], in0=v_bank[m][:, :], scalar=bv[:, m:m + 1], in1=attn[:, :],
                    op0=ALU.add, op1=ALU.mult).then_inc(context_ready, 1)
                if m >= 1:
                    lo_of_context(c, b, m - 1)
                if m == MT - 1:
                    lo_of_context(c, b, m)

            def step(c, b):
                split_scores(c, b)
                clip_scores(c)
                for m in range(MT):
                    context_tile(c, b, m)

            def add_output(c, n):
                wait(dve, o_done, NT * c + n + 1)
                x_tile = x_chunk(c, n, 1)
                nc.vector.scalar_tensor_tensor(
                    out=x_tile, in0=o_bank[n % 2][:, :], scalar=bo[:, n:n + 1], in1=x_tile,
                    op0=ALU.add, op1=ALU.add).then_inc(out_ready, 1)

            nc.vector.memset(context[:, 0, :], 0.0).then_inc(warm_ready, 1)
            first_lo(0)
            first_lo(1)
            dve.wait_ge(small_loaded, 48)
            dve.wait_ge(zeros_ready, 4)
            nc.vector.tensor_copy(cond_parts[:, :, 0:BATCH], cond[:, :, :]).then_inc(cond_hi_ready, 1)
            dve.wait_ge(cond_hi_ready, 1)
            lo_part(cond_parts[:, :, BATCH:2 * BATCH], cond[:, :, :], cond_parts[:, :, 0:BATCH]).then_inc(cond_ready, 1)
            for k in range(KT):
                dve.wait_ge(wq_hi_ready, k + 1)
                lo_part(wq_lo[:, k, :], wq_raw[:, k, :], wq_hi[:, k, :]).then_inc(wq_lo_ready, 1)
            first_lo(2)
            for m in range(MT):
                dve.wait_ge(wk_hi_ready, m + 1)
                lo_part(wk_lo[:, m, :], wk_raw[:, m, :], wk_hi[:, m, :]).then_inc(wk_lo_ready, 1)
            dve.wait_ge(q_done, 1)
            nc.vector.tensor_tensor(q_sum[:, :, :], q_psum, bq.unsqueeze(2).to_broadcast([P, MT, BATCH]),
                                    ALU.add).then_inc(q_sum_ready, 1)
            dve.wait_ge(q_sum_ready, 1)
            nc.vector.scalar_tensor_tensor(
                out=q_heads[:, :, :].rearrange("p m (b h) -> p (m b) h", b=BATCH),
                in0=q_sum[:, :, :].rearrange("p m b -> p (m b)").unsqueeze(2).to_broadcast([P, MT * BATCH, HEADS]),
                scalar=SCALE, in1=const[:, C_HEAD:C_HEAD + HEADS].unsqueeze(1).to_broadcast([P, MT * BATCH, HEADS]),
                op0=ALU.mult, op1=ALU.mult).then_inc(q_ready, 1)
            dve.wait_ge(q_ready, 1)
            nc.vector.tensor_copy(q_parts[:, :, 0:BATCH * HEADS], q_heads[:, :, :]).then_inc(q_hi_ready, 1)
            dve.wait_ge(q_hi_ready, 1)
            lo_part(q_parts[:, :, BATCH * HEADS:2 * BATCH * HEADS], q_heads[:, :, :],
                    q_parts[:, :, 0:BATCH * HEADS]).then_inc(q_parts_ready, 1)
            nc.vector.scalar_tensor_tensor(
                out=bk_q[:, :, :], in0=q_sum[:, :, :], scalar=SCALE,
                in1=bk.unsqueeze(2).to_broadcast([P, MT, BATCH]), op0=ALU.mult, op1=ALU.mult).then_inc(q_ready, 1)
            first_lo(3)
            lo_of_x(1, 1, 0)
            dve.wait_ge(a_done, 1)
            a_by_batch = a_psum.rearrange("p k (b h) -> p k b h", b=BATCH)
            for b in range(BATCH):
                if b == 1:
                    lo_of_x(1, 1, 1)
                twice = a_by_batch[:, :, b, :].unsqueeze(2).to_broadcast([P, KT, 2, HEADS])
                for to in (a_for_hi, a_for_lo):
                    nc.vector.tensor_copy(to[:, b, :, ROW_HI:ROW_LO + HEADS].rearrange("p k (s h) -> p k s h", s=2),
                                          twice).then_inc(a_ready, 1)
                dve.wait_ge(a_ready, 3 * b + 1)
                lo_part(a_for_hi[:, b, :, ROW_SMALL:ROW_SMALL + HEADS], a_by_batch[:, :, b, :],
                        a_for_hi[:, b, :, ROW_HI:ROW_HI + HEADS]).then_inc(a_ready, 1)
            dve.wait_ge(c_done, 1)
            nc.vector.tensor_reduce(c_score[:, :], c_psum.rearrange("p m b -> p b m"), mybir.AxisListType.X,
                                    ALU.add).then_inc(c_ready, 1)

            split_scores(0, 0)
            clip_scores(0)
            context_tile(0, 0, 0)
            context_tile(0, 0, 1)
            split_scores(1, 1)
            context_tile(0, 0, 2)
            context_tile(0, 0, 3)
            for m in range(MT):
                dve.wait_ge(wo_hi_ready, m + 1)
                lo_part(wo_lo[:, m, :], wo_raw[:, m, :], wo_hi[:, m, :]).then_inc(wo_lo_ready, 1)
            clip_scores(1)
            for m in range(MT):
                context_tile(1, 1, m)
            with dve.Fori(0, PER_BATCH - 1) as i:
                for b in range(BATCH):
                    c = 2 * i + 2 + b
                    add_output(c - 2, 0)
                    lo_of_x(c, b, 0)
                    add_output(c - 2, 1)
                    lo_of_x(c, b, 1)
                    for n in range(2, NT):
                        add_output(c - 2, n)
                    step(c, b)
            for n in range(NT):
                add_output(CHUNKS - 2, n)
            for n in range(NT - 1):
                add_output(CHUNKS - 1, n)
            for half in range(2):
                dve.wait_ge(o_done, NT * CHUNKS + half)
                x_half = x_all[:, bass.ds(CHUNKS * CHUNK - ROWS + half * ROWS // 2, ROWS // 2)]
                nc.vector.scalar_tensor_tensor(
                    out=x_half, in0=o_bank[1 - half][:, 0:ROWS // 2], scalar=bo[:, NT - 1:NT], in1=x_half,
                    op0=ALU.add, op1=ALU.add).then_inc(out_ready, 1)


def constant_columns():
    const = np.zeros((P, C_ALL), np.float32)
    p = np.arange(P)
    head = p // REP
    for first in (ROW_HI, ROW_LO, ROW_SMALL):
        const[first:first + HEADS, C_SELECT:C_SELECT + P] = np.arange(HEADS)[:, None] == head[None, :]
    const[:, C_SAME:C_SAME + P] = head[:, None] == head[None, :]
    const[:, C_HEAD:C_HEAD + HEADS] = head[:, None] == np.arange(HEADS)[None, :]
    const[ROW_LO:ROW_LO + HEADS, C_LO] = -1.0
    for first in (0, BATCH * HEADS):
        const[first:first + BATCH * HEADS, C_FOLD:C_FOLD + BATCH * HEADS] = np.eye(BATCH * HEADS)
    for first in (0, BATCH):
        const[first:first + BATCH, C_PAIR:C_PAIR + BATCH] = np.eye(BATCH)
    return const


def by_value_tile(w):
    w = w.reshape(HEADS, MT, REP, *w.shape[1:])
    return np.moveaxis(w, 1, 2).reshape(P, MT, *w.shape[3:])


def kernel(x, cond_1024, L0_cond_Wq, L0_cond_bq, L0_cond_Wk, L0_cond_bk, L0_cond_Wv, L0_cond_bv, L0_cond_Wo,
           L0_cond_bo):
    import concourse.bacc as bacc
    from concourse.bass_utils import run_bass_kernel_spmd

    x, cond, Wq, bq, Wk, bk, Wv, bv, Wo, bo = (
        np.asarray(a) for a in (x, cond_1024, L0_cond_Wq, L0_cond_bq, L0_cond_Wk, L0_cond_bk, L0_cond_Wv,
                                L0_cond_bv, L0_cond_Wo, L0_cond_bo))

    def in_by_out(w):
        w = by_value_tile(w).reshape(P, MT, KT, P)
        return w.transpose(3, 2, 1, 0).reshape(P, KT, D)

    laid = {
        "x_t": x.reshape(BATCH, PER_BATCH, ROWS, KT, P).transpose(1, 0, 4, 3, 2).reshape(CHUNKS, P, CHUNK),
        "wv_t": in_by_out(Wv),
        "wo_t": by_value_tile(Wo.T),
        "wq_t": in_by_out(Wq),
        "wk_t": by_value_tile(Wk),
        "cond_t": cond.reshape(BATCH, KT, P).transpose(2, 1, 0),
        "columns": np.stack([by_value_tile(bq), by_value_tile(bk), by_value_tile(bv), bo.reshape(NT, P).T], axis=1),
        "constants": constant_columns(),
    }
    laid = {name: np.ascontiguousarray(a) for name, a in laid.items()}
    nc = bacc.Bacc("TRN2", target_bir_lowering=False, num_devices=1)
    ins = [nc.dram_tensor(name, a.shape, mybir.dt.from_np(a.dtype), kind="ExternalInput").ap()
           for name, a in laid.items()]
    out = nc.dram_tensor("out_t", (CHUNKS, P, CHUNK), F32, kind="ExternalOutput").ap()
    build(nc, *ins, out)
    r = run_bass_kernel_spmd(nc, [laid], core_ids=[0])
    out = r.results[0]["out_t"].reshape(PER_BATCH, BATCH, P, NT, ROWS)
    return out.transpose(1, 0, 4, 3, 2).reshape(BATCH, LEN, D)
```
